# Optimizing a Trainium2 kernel written in Bass

```python
import numpy as np
import jax
import jax.numpy as jnp

def _softmax(x, axis=-1):
    return jax.nn.softmax(x, axis=axis)

def _gelu(x):
    return jax.nn.gelu(x, approximate=True)

def _silu(x):
    return jax.nn.silu(x)

def _sigmoid(x):
    return jax.nn.sigmoid(x)

def _layernorm(x, axis=-1, eps=1e-05):
    m = jnp.mean(x, axis=axis, keepdims=True)
    v = jnp.var(x, axis=axis, keepdims=True)
    return (x - m) / jnp.sqrt(v + eps)

def _scatter_add(tgt, idx, src, axis=0):
    return tgt.at[idx].add(src)

def _segment_sum(src, seg, n):
    return jax.ops.segment_sum(src, seg, n)
kernel_name = 'mk_rec_standalone_d1_rec_r8_ef249e'

def setup_inputs(seed: int=0):
    np.random.seed(seed)
    _w = jnp.asarray

    def _rec_inputs():
        import jax
        import jax.numpy as jnp
        _rk = jax.random.key(seed)
        r_q = -9.80646e-05 + 1.00041 * jax.random.normal(jax.random.fold_in(_rk, 1), (2048, 128), jnp.float32)
        r_k = -9.97791e-05 + 0.999858 * jax.random.normal(jax.random.fold_in(_rk, 2), (2048, 200, 128), jnp.float32)
        r_mask = jax.random.randint(jax.random.fold_in(_rk, 3), (2048, 200), 0, 2, jnp.int32)
        return (r_q, r_k, r_mask)
    r_q, r_k, r_mask = _rec_inputs()

    def _L0_rec_setup():
        import jax, jax.numpy as jnp
        import numpy as np
        B, L, D, H = (512, 200, 128, 64)
        NEG = -1000000000.0
        key = jax.random.key(seed)
        ks = jax.random.split(key, 6)
        q = jax.random.normal(ks[0], (B, D), dtype=jnp.float32)
        k = jax.random.normal(ks[1], (B, L, D), dtype=jnp.float32)
        mask = jax.random.randint(ks[2], (B, L), 0, 2, dtype=jnp.int32)
        W1 = jax.random.normal(ks[3], (4 * D, H), dtype=jnp.float32) * (1.0 / np.sqrt(4 * D))
        b1 = jnp.zeros((H,), dtype=jnp.float32)
        alpha = jnp.full((1,), 0.25, dtype=jnp.float32)
        W2 = jax.random.normal(ks[4], (H, 1), dtype=jnp.float32) * (1.0 / np.sqrt(H))
        b2 = jnp.zeros((1,), dtype=jnp.float32)
        return {'q': q, 'k': k, 'mask': mask, 'W1': W1, 'b1': b1, 'alpha': alpha, 'W2': W2, 'b2': b2}
    _L0_rec_all = _L0_rec_setup()
    _L0_rec_in = {k: v for k, v in _L0_rec_all.items() if k in ('W1', 'b1', 'alpha', 'W2', 'b2')}
    del _L0_rec_all
    return {'r_q': r_q, 'r_k': r_k, 'r_mask': r_mask, 'L0_rec_W1': _L0_rec_in['W1'], 'L0_rec_b1': _L0_rec_in['b1'], 'L0_rec_alpha': _L0_rec_in['alpha'], 'L0_rec_W2': _L0_rec_in['W2'], 'L0_rec_b2': _L0_rec_in['b2']}

def reference(r_q, r_k, r_mask, L0_rec_W1, L0_rec_b1, L0_rec_alpha, L0_rec_W2, L0_rec_b2):
    import jax
    import jax.numpy as jnp

    def _L0_rec_ref(q, k, mask, W1, b1, alpha, W2, b2):
        import jax, jax.numpy as jnp
        import numpy as np
        B, L, D, H = (512, 200, 128, 64)
        NEG = -1000000000.0
        qe = jnp.broadcast_to(q[:, None, :], k.shape)
        feat = jnp.concatenate([qe, k, qe - k, qe * k], axis=-1)
        h = feat @ W1 + b1
        h = jnp.where(h >= 0, h, alpha[0] * h)
        a = (h @ W2 + b2)[..., 0]
        a = jnp.where(mask == 0, jnp.float32(NEG), a)
        w = jax.nn.softmax(a, axis=-1)
        return jnp.einsum('bl,bld->bd', w, k)
    y = _L0_rec_ref(r_q, r_k, r_mask, L0_rec_W1, L0_rec_b1, L0_rec_alpha, L0_rec_W2, L0_rec_b2)
    return y

_drawn_inputs = setup_inputs


def setup_inputs(seed=0):
    import zlib

    import numpy as np

    out = dict(_drawn_inputs(seed))
    spreads = {'L0_rec_b1': (0.0, 0.275)}
    factors = {}
    for name, (base, spread) in spreads.items():
        noise = np.random.default_rng([zlib.crc32(name.encode()), seed]).standard_normal(out[name].shape)
        drawn = base * np.exp(spread * noise) if base else spread * noise
        out[name] = jnp.asarray(drawn.astype(out[name].dtype))
    for name, factor in factors.items():
        out[name] = (out[name] * factor).astype(out[name].dtype)
    return out
```

```python
from contextlib import ExitStack

import concourse.bass as bass
from concourse import mybir

F32 = mybir.dt.float32
I32 = mybir.dt.int32
ALU = mybir.AluOpType
ACT = mybir.ActivationFunctionType
AX_X = mybir.AxisListType.X

P = 128
B, L, D, H = 2048, 200, 128, 64
SUB = 16
KP = P // SUB
J = L // KP
TILES = B // SUB
GT = 4
GB = GT * SUB
GROUPS = TILES // GT
SLOTS = 8
LAG = 5
PAIRS = SUB // 2
PHASES = 4
BATCH = 4
BATCHES = [(j, min(j + BATCH, J)) for j in range(0, J, BATCH)]
NB = len(BATCHES)
QUADS = 4
QP = P // QUADS
HALF_Q = QP // 2
NEG = -1000000000.0
POOL_CUTS = [0, 7, 13, 19, 25]


def ge(eng, sem, value):
    if not isinstance(value, int) or value > 0:
        eng.wait_ge(sem, value)


def run_steps(eng, step):
    for s in range(SLOTS):
        step(0, s)
    with eng.Fori(1, TILES // SLOTS - 1) as it:
        for s in range(SLOTS):
            step(it, s)
    for n in range(TILES - SLOTS, TILES + LAG + 1):
        step(n // SLOTS, n % SLOTS)


def tile_at(it, s, back=0):
    at = s - back
    return it * SLOTS + at, at % SLOTS, it * (SLOTS // GT) + at // GT, at % GT


def round_of(it, s, back=0):
    return it + (s - back) // SLOTS


def inside(n, least, end):
    return not isinstance(n, int) or least <= n < end


def attention_pooling(nc, r_q, r_k, r_mask, W1, b1, alpha, W2, b2, out):
    k_tiles = r_k.rearrange("(n b) (i j) d -> n (b i) (j d)", b=SUB, i=KP)
    mask_rows = r_mask.rearrange("(g v c) l -> g c v l", v=HALF_Q, c=QUADS)
    out_rows = out.rearrange("(g s p) d -> g p s d", s=GT, p=SUB)
    probs_dram = nc.dram_tensor("probs_scratch", [B, L], F32, kind="Internal").ap()
    probs_rows = probs_dram.rearrange("(g v c) l -> g c v l", v=HALF_Q, c=QUADS)
    probs_tiles = probs_dram.rearrange("(g s b) (i j) -> g (b i) s j", s=GT, b=SUB, i=KP)

    with ExitStack() as ctx:
        def sb(name, shape, dt=F32):
            return ctx.enter_context(nc.sbuf_tensor(name, shape, dt))

        def ps(name, shape):
            return ctx.enter_context(nc.psum_tensor(name, shape, F32))

        def sem(name):
            return ctx.enter_context(nc.semaphore(name))

        keys = sb("keys", [P, SLOTS, J * D])
        keysT = sb("keysT", [P, 2, J * P])
        weff = sb("weff", [P, 2, SUB, H])
        weff_q = sb("weff_q", [P, SUB, H])
        hidden = sb("hidden", [P, 2, PAIRS // 2, L])
        act = sb("act", [P, 2, PAIRS // 2, L])
        masks = sb("masks", [P, 2, L], I32)
        masked = sb("masked", [P, 2, L], I32)
        logits = sb("logits", [P, L])
        expd = sb("expd", [P, L])
        probs = sb("probs", [P, 2, L])
        probs_k = sb("probs_k", [P, 2, GT, J])
        pool_w = sb("pool_w", [P, 2, J, SUB])
        parts = sb("parts", [P, 2, D])
        pooled = sb("pooled", [SUB, 2, GT * D])
        neg_max = sb("neg_max", [P, 1])
        exp_sum = sb("exp_sum", [P, 1])
        inv_sum = sb("inv_sum", [P, 1])
        ident = sb("ident", [P, P])
        own_b = sb("own_b", [P, SUB])
        quad_b = sb("quad_b", [P, SUB])
        neg = sb("neg", [P, L])
        q_sb = sb("q_sb", [P, B // P, D])
        qT = sb("qT", [P, B])
        w1 = sb("w1", [P, 4, H])
        wq_f = sb("wq_f", [P, H])
        wk_f = sb("wk_f", [P, H])
        wp_f = sb("wp_f", [P, H])
        wsum = sb("wsum", [P, 2, H])
        al = sb("al", [P, 1])
        sgn2 = sb("sgn2", [P, 1])
        sgn = sb("sgn", [P, 1])
        b1c = sb("b1c", [P, 1])
        b1s = sb("b1s", [P, 1])
        b2c = sb("b2c", [P, 1])
        w2c = sb("w2c", [P, 1])
        w2win = sb("w2win", [P, 2 * HALF_Q - 2])
        bias = sb("bias", [P, B // 2])

        trP = [ps(f"trP{x}", [P, BATCH * P]) for x in range(2)]
        hP = [ps(f"hP{x}", [P, 512]) for x in range(2)]
        scoreP = ps("scoreP", [P, 512])
        partP = ps("partP", [P, 512])
        pooledP = ps("pooledP", [P, 512])

        keys_in = [sem(f"keys_in{x}") for x in range(SLOTS)]
        mask_in = [sem(f"mask_in{x}") for x in range(2)]
        params_in = sem("params_in")
        consts_done = sem("consts_done")
        consts_base = sem("consts_base")
        zeroed = sem("zeroed")
        fold = sem("fold")
        qT_trans = sem("qT_trans")
        qT_done = sem("qT_done")
        bias_mm = sem("bias_mm")
        setup_done = sem("setup_done")
        trans_done = sem("trans_done")
        keysT_done = sem("keysT_done")
        weffq_done = sem("weffq_done")
        weff_done = sem("weff_done")
        main_done = sem("main_done")
        hidden_done = sem("hidden_done")
        act_done = sem("act_done")
        score_done = sem("score_done")
        logits_read = sem("logits_read")
        mask_ready = sem("mask_ready")
        logits_masked = sem("logits_masked")
        max_done = sem("max_done")
        exp_done = sem("exp_done")
        inv_done = sem("inv_done")
        probs_done = sem("probs_done")
        probs_out = sem("probs_out")
        probs_in = [sem(f"probs_in{x}") for x in range(2)]
        poolw_done = sem("poolw_done")
        part_done = sem("part_done")
        parts_done = sem("parts_done")
        pooled_done = sem("pooled_done")
        pooled_moved = sem("pooled_moved")
        out_done = [sem(f"out_done{x}") for x in range(2)]

        PARAMS = 9 * 16
        CONSTS = 4 + QUADS + 2

        block = ctx.enter_context(nc.Block())

        @block.sync
        def _(sp):
            def load_keys(n, s):
                sp.dma_start(keys[:, s, :], k_tiles[n]).then_inc(keys_in[s], 16)

            def load_mask(g, x):
                for c in range(QUADS):
                    sp.dma_start(masks[QP * c:QP * c + HALF_Q, x, :],
                                 mask_rows[g, c]).then_inc(mask_in[x], 16)

            sp.dma_start(w1[:], W1.rearrange("(c p) h -> p c h", p=P)).then_inc(params_in, 16)
            sp.dma_start(al[:], alpha.rearrange("(a b) -> a b", b=1).broadcast_to([P, 1])).then_inc(params_in, 16)
            sp.dma_start(b2c[:], b2.rearrange("(a b) -> a b", b=1).broadcast_to([P, 1])).then_inc(params_in, 16)
            for r in range(2):
                sp.dma_start(b1c[H * r:H * r + H, :], b1.rearrange("(a b) -> a b", b=1)).then_inc(params_in, 16)
                sp.dma_start(w2c[H * r:H * r + H, :], W2).then_inc(params_in, 16)
            q_v = r_q.rearrange("(t p) d -> p t d", p=P)
            load_keys(0, 0)
            for h in range(2):
                sp.dma_start(q_sb[:, 8 * h:8 * h + 8, :], q_v[:, 8 * h:8 * h + 8, :]).then_inc(params_in, 16)
            for n in range(1, SLOTS):
                load_keys(n, n)
                if n == 2:
                    sp.wait_ge(zeroed, 1)
                    load_mask(0, 0)
                    load_mask(1, 1)

            def step(it, s):
                n = tile_at(it, s)[0]
                if s % GT == 0 and inside(n, GT, TILES + 1):
                    g, x = tile_at(it, s, GT)[2], (s // GT + 1) % 2
                    ge(sp, poolw_done, (g - 1) * GT)
                    ge(sp, probs_done, g + 1)
                    for c in range(QUADS):
                        sp.dma_start(probs_rows[g, c],
                                     probs[QP * c:QP * c + HALF_Q, x, :]
                                     ).then_inc(probs_out, 16)
                    ge(sp, probs_out, (g + 1) * (16 * QUADS))
                    sp.dma_start(probs_k[:, x, :, :], probs_tiles[g]).then_inc(probs_in[x], 16)
                if s % GT == 2 and inside(n, GT, TILES - GT):
                    g, x = tile_at(it, s)[2] + 1, (s // GT + 1) % 2
                    ge(sp, mask_ready, g - 1)
                    sp.wait_ge(zeroed, 1)
                    load_mask(g, x)
                if inside(n, LAG, TILES - SLOTS + LAG):
                    ge(sp, part_done, n - LAG + 1)
                    load_keys(n - LAG + SLOTS, (s - LAG) % SLOTS)
                if (s - LAG - 1) % GT == GT - 1 and inside(n, LAG + GT, TILES + LAG + 1):
                    g, x = tile_at(it, s, LAG + 1)[2], (s - LAG - 1) % SLOTS // GT
                    ge(sp, pooled_moved, g + 1)
                    sp.dma_start(out_rows[g], pooled[:, x, :].rearrange("p (s d) -> p s d", s=GT)
                                 ).then_inc(out_done[x], 16)

            run_steps(sp, step)
            for x in range(2):
                sp.wait_ge(out_done[x], 16 * (GROUPS // 2))

        @block.gpsimd
        def _(pool):
            g_ = nc.gpsimd
            g_.memset(ident[:], 0.0).then_inc(consts_base, 1)
            g_.memset(own_b[:], 1.0).then_inc(consts_base, 1)
            g_.memset(quad_b[:], 0.0).then_inc(consts_base, 1)
            g_.memset(neg[:], NEG).then_inc(consts_done, 1)
            pool.wait_ge(consts_base, 3)
            g_.affine_select(out=ident[:], in_=ident[:], compare_op=ALU.not_equal, fill=1.0, base=0,
                             pattern=[[-1, P]], channel_multiplier=1).then_inc(consts_done, 1)
            g_.affine_select(out=own_b[:], in_=own_b[:], compare_op=ALU.is_ge, fill=0.0, base=0,
                             pattern=[[-KP, SUB]], channel_multiplier=1).then_inc(consts_base, 1)
            pool.wait_ge(consts_base, 4)
            g_.affine_select(out=own_b[:], in_=own_b[:], compare_op=ALU.is_ge, fill=0.0, base=KP - 1,
                             pattern=[[KP, SUB]], channel_multiplier=-1).then_inc(consts_done, 1)
            for c in range(QUADS):
                if c:
                    pool.wait_ge(consts_base, 4 + c)
                g_.affine_select(out=quad_b[:], in_=quad_b[:], compare_op=ALU.not_equal, fill=1.0,
                                 base=-QP * c, pattern=[[-1, SUB]], channel_multiplier=1
                                 ).then_inc(consts_base if c < QUADS - 1 else consts_done, 1)
            pool.wait_ge(setup_done, 1)

            def weights(n, x):
                if isinstance(n, int):
                    q_n = qT[:, n * SUB:(n + 1) * SUB]
                else:
                    q_n = qT[:, bass.ds(n * SUB, SUB)]
                ge(pool, weff_done, n)
                g_.tensor_tensor(weff_q[:], q_n.unsqueeze(2).broadcast_to([P, SUB, H]),
                                 wp_f[:].unsqueeze(1).broadcast_to([P, SUB, H]), ALU.mult
                                 ).then_inc(weffq_done, 1)
                ge(pool, weffq_done, n + 1)
                ge(pool, main_done, (n - 1) * PHASES)
                g_.tensor_tensor(weff[:, x, :, :], weff_q[:], wk_f[:].unsqueeze(1).broadcast_to([P, SUB, H]),
                                 ALU.add).then_inc(weff_done, 1)

            weights(0, 0)

            def step(it, s):
                n = tile_at(it, s)[0]
                if inside(n, LAG, TILES + LAG):
                    m, ms, _, sg = tile_at(it, s, LAG)
                    x = ms // GT % 2
                    if sg == 0:
                        pool.wait_ge(probs_in[x], (round_of(it, s, LAG) + 1) * 16)
                    ge(pool, part_done, m - 1)
                    g_.tensor_tensor(pool_w[:, ms % 2, :, :],
                                     probs_k[:, x, sg, :].unsqueeze(2).broadcast_to([P, J, SUB]),
                                     own_b[:].unsqueeze(1).broadcast_to([P, J, SUB]), ALU.mult
                                     ).then_inc(poolw_done, 1)
                if inside(n, 0, TILES - 1):
                    weights(n + 1, (s + 1) % 2)
            run_steps(pool, step)

        @block.scalar
        def _(act_e):
            a_ = nc.scalar
            act_e.wait_ge(setup_done, 1)

            def hidden_pairs(n, s, q):
                ge(act_e, main_done, n * PHASES + q + 1)
                for k in range(2):
                    u = 2 * q + k
                    a, v = u // (PAIRS // 2), u % (PAIRS // 2)
                    if v == 0:
                        ge(act_e, act_done, 2 * n + a - 1)
                    if isinstance(n, int):
                        bias_u = bias[:, n * PAIRS + u:n * PAIRS + u + 1]
                    else:
                        bias_u = bias[:, bass.ds(n * PAIRS + u, 1)]
                    a_.activation(hidden[:, a, v, :], hP[q % 2][:, k * L:(k + 1) * L], ACT.Identity,
                                  bias=bias_u).then_inc(hidden_done, 1)

            def step(it, s):
                n = tile_at(it, s)[0]
                if inside(n, LAG + 1, TILES + LAG + 1):
                    m, ms, _, _ = tile_at(it, s, LAG + 1)
                    ge(act_e, part_done, m + 1)
                    ge(act_e, pooled_done, m - 1)
                    a_.activation(parts[:, ms % 2, :], partP[:, 0:D], ACT.Copy).then_inc(parts_done, 1)
                for q in range(PHASES):
                    if inside(n, 0, TILES):
                        hidden_pairs(n, s, q)
                    if q == 1 and s % GT == 0 and inside(n, GT, TILES + 1):
                        g = tile_at(it, s, GT)[2]
                        ge(act_e, max_done, g + 1)
                        ge(act_e, probs_done, g)
                        a_.activation(expd[:], logits[:], ACT.Exp, bias=neg_max[:], accum_out=exp_sum[:]
                                      ).then_inc(exp_done, 1)
                    if q == 1 and (s - LAG - 1) % GT == GT - 1 and inside(n, LAG + GT, TILES + LAG + 1):
                        _, ms, g, _ = tile_at(it, s, LAG + 1)
                        x = ms // GT % 2
                        ge(act_e, pooled_done, (g + 1) * GT)
                        ge(act_e, out_done[x], round_of(it, s, LAG + 1) * 16)
                        a_.activation(pooled[:, x, :], pooledP[0:SUB, :], ACT.Copy).then_inc(pooled_moved, 1)

            run_steps(act_e, step)

        @block.vector
        def _(dve):
            v_ = nc.vector
            v_.memset(scoreP[:], 0.0)
            v_.memset(partP[:], 0.0)
            v_.memset(w2win[:], 0.0).then_inc(fold, 1)
            v_.memset(masks[:].rearrange("p a l -> p (a l)"), 0).then_inc(zeroed, 1)
            dve.wait_ge(params_in, PARAMS)
            v_.tensor_scalar(sgn2[:], al[:], 1.0, 2.0, ALU.is_le, ALU.mult).then_inc(fold, 1)
            v_.tensor_tensor(wsum[:, 0, :], w1[:, 0, :], w1[:, 2, :], ALU.add).then_inc(fold, 1)
            v_.tensor_tensor(wsum[:, 1, :], w1[:, 1, :], w1[:, 2, :], ALU.subtract).then_inc(fold, 1)
            dve.wait_ge(fold, 4)
            v_.tensor_scalar(sgn[:], sgn2[:], 1.0, None, ALU.subtract).then_inc(fold, 1)
            dve.wait_ge(fold, 5)
            v_.tensor_scalar(wq_f[:], wsum[:, 0, :], sgn[:], None, ALU.mult)
            v_.tensor_scalar(wk_f[:], wsum[:, 1, :], sgn[:], None, ALU.mult)
            v_.tensor_scalar(wp_f[:], w1[:, 3, :], sgn[:], None, ALU.mult)
            v_.tensor_scalar(b1s[:], b1c[:], sgn[:], None, ALU.mult)
            for r in range(2):
                v_.tensor_scalar(w2win[H * r:H * r + H, HALF_Q - 2 + r:HALF_Q - 1 + r],
                                 w2c[H * r:H * r + H, :], sgn[H * r:H * r + H, :], None, ALU.mult
                                 ).then_inc(fold, 1)
            for t in range(B // P // BATCH):
                dve.wait_ge(qT_trans, t + 1)
                v_.tensor_copy(qT[:, t * BATCH * P:(t + 1) * BATCH * P], trP[t % 2][:]).then_inc(qT_done, 1)
            for c in range(2):
                dve.wait_ge(bias_mm, c + 1)
                v_.tensor_scalar(bias[:, c * 512:(c + 1) * 512], hP[c][:], b1s[:], None, ALU.add
                                 ).then_inc(fold, 1)
            dve.wait_ge(fold, 9)
            dve.wait_ge(consts_done, 4)
            v_.tensor_copy(sgn2[:], sgn[:]).then_inc(setup_done, 1)

            def move_batch(n, s, b):
                if b == 0:
                    ge(dve, main_done, (n - 1) * PHASES)
                ge(dve, trans_done, n * NB + b + 1)
                j0, j1 = BATCHES[b]
                v_.tensor_copy(keysT[:, s % 2, j0 * P:j1 * P], trP[(s * NB + b) % 2][:, 0:(j1 - j0) * P]
                               ).then_inc(keysT_done, 1)

            def activate(n, s, a):
                ge(dve, hidden_done, (2 * n + a + 1) * (PAIRS // 2))
                ge(dve, score_done, 2 * n + a - 1)
                h_ = hidden[:, a, :, :].rearrange("p v l -> p (v l)")
                v_.scalar_tensor_tensor(act[:, a, :, :].rearrange("p v l -> p (v l)"), h_, al[:], h_,
                                        ALU.mult, ALU.max).then_inc(act_done, 1)

            def mask_scores(g, x):
                ge(dve, score_done, (g + 1) * (2 * GT))
                ge(dve, exp_done, g)
                v_.tensor_scalar(logits[:].rearrange("p (i j) -> p j i", i=KP),
                                 scoreP[:, 0:L].rearrange("p (j i) -> p j i", i=KP), b2c[:], None, ALU.add
                                 ).then_inc(logits_read, 1)
                dve.wait_ge(consts_done, 1)
                ge(dve, logits_read, g + 1)
                ge(dve, mask_ready, g + 1)
                v_.copy_predicated(logits[:], masked[:, x, :], neg[:]).then_inc(logits_masked, 1)
                ge(dve, logits_masked, g + 1)
                v_.tensor_reduce(neg_max[:], logits[:], AX_X, ALU.max, negate=True).then_inc(max_done, 1)

            def normalise(g, x):
                ge(dve, exp_done, g + 1)
                v_.reciprocal(inv_sum[:], exp_sum[:]).then_inc(inv_done, 1)
                ge(dve, inv_done, g + 1)
                ge(dve, probs_out, (g - 1) * (16 * QUADS))
                v_.tensor_scalar(probs[:, x, :], expd[:], inv_sum[:], None, ALU.mult).then_inc(probs_done, 1)

            for b in range(NB):
                move_batch(0, 0, b)

            def step(it, s):
                n = tile_at(it, s)[0]
                scored = s % GT == 0 and inside(n, GT, TILES + 1)
                g, x = tile_at(it, s, GT)[2], (s // GT + 1) % 2
                for q in range(PHASES):
                    if inside(n, 0, TILES - 1):
                        for b in range(2 * q, min(2 * q + 2, NB)):
                            move_batch(n + 1, (s + 1) % SLOTS, b)
                    if q == 0 and scored:
                        mask_scores(g, x)
                    if q % 2 and inside(n, 0, TILES):
                        activate(n, s, q // 2)
                    if q == 2 and s % GT == 1 and inside(n, 0, TILES):
                        dve.wait_ge(mask_in[s // GT], (it + 1) * (16 * QUADS))
                        ge(dve, logits_masked, tile_at(it, s)[2] - 1)
                        v_.tensor_scalar(masked[:, s // GT, :], masks[:, s // GT, :], 0, None, ALU.is_equal
                                         ).then_inc(mask_ready, 1)
                    if q == 1 and scored:
                        normalise(g, x)

            run_steps(dve, step)

        @block.tensor
        def _(pe):
            t_ = nc.tensor
            pe.wait_ge(params_in, PARAMS)
            pe.wait_ge(consts_done, 4)
            for t in range(B // P):
                if t % BATCH == 0 and t >= 2 * BATCH:
                    pe.wait_ge(qT_done, t // BATCH - 1)
                mm = t_.transpose(trP[t // BATCH % 2][:, t % BATCH * P:(t % BATCH + 1) * P], q_sb[:, t, :],
                                  ident[:])
                if t % BATCH == BATCH - 1:
                    mm.then_inc(qT_trans, 1)
            pe.wait_ge(fold, 7)
            pe.wait_ge(qT_done, B // P // BATCH)
            for c in range(2):
                for r in range(2):
                    mm = t_.matmul(hP[c][H * r:H * r + H, :], wq_f[:],
                                   qT[:, 1024 * c:1024 * (c + 1)].rearrange("p (a r c) -> p r a c", r=2, c=QUADS)[:, r],
                                   start=True, stop=True)
                mm.then_inc(bias_mm, 1)

            def transpose_batch(n, s, rnd, b):
                if b == 0:
                    pe.wait_ge(keys_in[s], (rnd + 1) * 16)
                ge(pe, keysT_done, n * NB + b - 1)
                j0, j1 = BATCHES[b]
                for j in range(j0, j1):
                    mm = t_.transpose(trP[(s * NB + b) % 2][:, (j - j0) * P:(j - j0 + 1) * P],
                                      keys[:, s, j * D:(j + 1) * D], ident[:])
                mm.then_inc(trans_done, 1)

            def first_layer(n, s, q):
                if q == 0:
                    ge(pe, keysT_done, (n + 1) * NB)
                    ge(pe, weff_done, n + 1)
                ge(pe, hidden_done, 2 * (n * PHASES + q - 1))
                kT = keysT[:, s % 2, :].rearrange("p (j c) -> p j c", j=J)
                for k in range(2):
                    for r in range(2):
                        b = 8 * (q // 2) + 4 * r + 2 * (q % 2) + k
                        mm = t_.matmul(hP[q % 2][H * r:H * r + H, k * L:(k + 1) * L], weff[:, s % 2, b, :],
                                       kT[:, :, b * KP:(b + 1) * KP], start=True, stop=True)
                mm.then_inc(main_done, 1)

            def second_layer(n, s, g, a):
                ge(pe, act_done, 2 * n + a + 1)
                if s % GT == 0 and a == 0:
                    ge(pe, logits_read, g)
                t = 2 * (s % GT) + a
                for c in range(QUADS):
                    mm = t_.matmul(scoreP[QP * c:QP * c + HALF_Q, 0:L],
                                   w2win[:, HALF_Q - 2 - 2 * t:2 * HALF_Q - 2 - 2 * t],
                                   act[:, a, c, :], start=(t == 0), stop=(t == 2 * GT - 1))
                mm.then_inc(score_done, 1)

            def pool_keys(m, ms, q):
                if q == 0:
                    ge(pe, poolw_done, m + 1)
                    ge(pe, parts_done, m)
                for j in range(POOL_CUTS[q], POOL_CUTS[q + 1]):
                    c = j % QUADS
                    mm = t_.matmul(partP[QP * c:QP * c + SUB, 0:D], pool_w[:, ms % 2, j, :],
                                   keys[:, ms, j * D:(j + 1) * D], start=(j < QUADS), stop=(j + QUADS >= J))
                if q == PHASES - 1:
                    mm.then_inc(part_done, 1)

            def add_parts(m, ms, g):
                ge(pe, parts_done, m + 1)
                if ms % GT == 0:
                    ge(pe, pooled_moved, g)
                t_.matmul(pooledP[0:SUB, (ms % GT) * D:(ms % GT + 1) * D], quad_b[:], parts[:, ms % 2, :],
                          start=True, stop=True).then_inc(pooled_done, 1)

            pe.wait_ge(setup_done, 1)
            for b in range(NB):
                transpose_batch(0, 0, 0, b)

            def step(it, s):
                n = tile_at(it, s)[0]
                for q in range(PHASES):
                    if inside(n, 0, TILES - 1):
                        for b in range(2 * q, min(2 * q + 2, NB)):
                            transpose_batch(n + 1, (s + 1) % SLOTS, round_of(it, s, -1), b)
                    if inside(n, 0, TILES):
                        first_layer(n, s, q)
                    if q == 0 and inside(n, 1, TILES + 1):
                        second_layer(n - 1, (s - 1) % SLOTS, tile_at(it, s, 1)[2], 1)
                    if q == 2 and inside(n, 0, TILES):
                        second_layer(n, s, tile_at(it, s)[2], 0)
                    if q == 0 and inside(n, LAG + 1, TILES + LAG + 1):
                        add_parts(*tile_at(it, s, LAG + 1)[:3])
                    if inside(n, LAG, TILES + LAG):
                        pool_keys(n - LAG, (s - LAG) % SLOTS, q)

            run_steps(pe, step)


_INS = ["r_q", "r_k", "r_mask", "L0_rec_W1", "L0_rec_b1", "L0_rec_alpha", "L0_rec_W2", "L0_rec_b2"]


def kernel(**inputs):
    import numpy as np
    import concourse.bacc as bacc
    from concourse.bass_utils import run_bass_kernel_spmd

    nc = bacc.Bacc("TRN2", target_bir_lowering=False, num_devices=1)
    arrays, args = {}, []
    for name in _INS:
        a = np.ascontiguousarray(inputs[name])
        arrays[f"in_{name}"] = a
        args.append(nc.dram_tensor(f"in_{name}", a.shape, mybir.dt.from_np(a.dtype), kind="ExternalInput").ap())
    args.append(nc.dram_tensor("out_rows", (B, D), F32, kind="ExternalOutput").ap())
    attention_pooling(nc, *args)
    r = run_bass_kernel_spmd(nc, [arrays], core_ids=[0])
    return r.results[0]["out_rows"]
```

```python
from contextlib import ExitStack

import concourse.bass as bass
from concourse import mybir

F32 = mybir.dt.float32
I32 = mybir.dt.int32
ALU = mybir.AluOpType
ACT = mybir.ActivationFunctionType
AX_X = mybir.AxisListType.X

P = 128
B, L, D, H = 2048, 200, 128, 64
SUB = 16
KP = P // SUB
J = L // KP
TILES = B // SUB
GT = 4
GROUPS = TILES // GT
SLOTS = 8
LAG = 5
PAIRS = SUB // 2
PHASES = 4
BATCH = 4
BATCHES = [(j, min(j + BATCH, J)) for j in range(0, J, BATCH)]
NB = len(BATCHES)
QUADS = 4
QP = P // QUADS
HALF_Q = QP // 2
NEG = -1000000000.0
BY_DVE = [15, 17, 17, 13]
BY_DVE_LAST = 4
BANK = [0, 1, 2, 0, 1, 2, 0]
PHASE_BATCHES = [[0, 1, 2], [3, 4], [5, 6], []]


def ge(eng, sem, value):
    if not isinstance(value, int) or value > 0:
        eng.wait_ge(sem, value)


def run_steps(eng, step):
    for s in range(SLOTS):
        step(0, s)
    with eng.Fori(1, TILES // SLOTS - 1) as it:
        for s in range(SLOTS):
            step(it, s)
    for n in range(TILES - SLOTS, TILES + LAG + 1):
        step(n // SLOTS, n % SLOTS)


def tile_at(it, s, back=0):
    at = s - back
    return it * SLOTS + at, at % SLOTS, it * (SLOTS // GT) + at // GT, at % GT


def round_of(it, s, back=0):
    return it + (s - back) // SLOTS


def by_dve(m, ms):
    return BY_DVE_LAST if isinstance(m, int) and m >= TILES - GT else BY_DVE[ms % GT]


def inside(n, least, end):
    return not isinstance(n, int) or least <= n < end


def attention_pooling(nc, r_q, r_k, r_mask, W1, b1, alpha, W2, b2, out):
    k_tiles = r_k.rearrange("(n b) (i j) d -> n (b i) (j d)", b=SUB, i=KP)
    mask_rows = r_mask.rearrange("(g s c w) l -> g c s w l", s=GT, c=QUADS, w=SUB // QUADS)
    out_rows = out.rearrange("(g s p) d -> g p s d", s=GT, p=SUB)
    probs_dram = nc.dram_tensor("probs_scratch", [2, P, L], F32, kind="Internal").ap()
    probs_tiles = probs_dram.rearrange("x (c h s w) (i j) -> x h s c (w i) j", c=QUADS, h=2, s=GT, i=KP)[:, 0]

    with ExitStack() as ctx:
        def sb(name, shape, dt=F32):
            return ctx.enter_context(nc.sbuf_tensor(name, shape, dt))

        def ps(name, shape):
            return ctx.enter_context(nc.psum_tensor(name, shape, F32))

        def sem(name):
            return ctx.enter_context(nc.semaphore(name))

        keys = sb("keys", [P, SLOTS, J * D])
        keysT = sb("keysT", [P, 2, J * P])
        weff = sb("weff", [P, 2, SUB, H])
        weff_q = sb("weff_q", [P, SUB, H])
        hidden = sb("hidden", [P, 2, PAIRS // 2, L])
        act = sb("act", [P, 2, PAIRS // 2, L])
        masks = sb("masks", [P, 2, L], I32)
        masked = sb("masked", [P, 2, L], I32)
        logits = sb("logits", [P, L])
        expd = sb("expd", [P, L])
        probs = sb("probs", [P, 2, L])
        probs_k = sb("probs_k", [P, 2, GT, J])
        pool_w = sb("pool_w", [P, 2, J - min(BY_DVE + [BY_DVE_LAST]), SUB])
        parts = sb("parts", [P, 2, D])
        products = sb("products", [P, max(BY_DVE) * D])
        parts_v = sb("parts_v", [P, 2, D])
        pooled = sb("pooled", [SUB, 2, GT * D])
        neg_max = sb("neg_max", [P, 1])
        exp_sum = sb("exp_sum", [P, 1])
        inv_sum = sb("inv_sum", [P, 1])
        ident = sb("ident", [P, P])
        own_b = sb("own_b", [P, SUB])
        quad_b = sb("quad_b", [P, SUB])
        neg = sb("neg", [P, L])
        q_sb = sb("q_sb", [P, B // P, D])
        qT = sb("qT", [P, B])
        w1 = sb("w1", [P, 4, H])
        wq_f = sb("wq_f", [P, H])
        wk_f = sb("wk_f", [P, H])
        wp_f = sb("wp_f", [P, H])
        wsum = sb("wsum", [P, 2, H])
        al = sb("al", [P, 1])
        sgn2 = sb("sgn2", [P, 1])
        sgn = sb("sgn", [P, 1])
        b1c = sb("b1c", [P, 1])
        b1s = sb("b1s", [P, 1])
        b2c = sb("b2c", [P, 1])
        w2c = sb("w2c", [P, 1])
        w2win = sb("w2win", [P, 2 * HALF_Q - 2])
        bias = sb("bias", [P, B // 2])

        trP = [ps(f"trP{x}", [P, BATCH * P]) for x in range(3)]
        hP = [ps(f"hP{x}", [P, 512]) for x in range(2)]
        scoreP = ps("scoreP", [P, 512])
        partP = ps("partP", [P, 512])
        pooledP = ps("pooledP", [P, 512])

        keys_in = [sem(f"keys_in{x}") for x in range(SLOTS)]
        mask_in = [sem(f"mask_in{x}") for x in range(2)]
        params_in = sem("params_in")
        consts_done = sem("consts_done")
        consts_base = sem("consts_base")
        zeroed = sem("zeroed")
        fold = sem("fold")
        qT_trans = sem("qT_trans")
        qT_done = sem("qT_done")
        bias_mm = sem("bias_mm")
        trans_done = sem("trans_done")
        keysT_done = sem("keysT_done")
        products_done = sem("products_done")
        parts_v_done = sem("parts_v_done")
        weffq_done = sem("weffq_done")
        weff_done = sem("weff_done")
        main_done = sem("main_done")
        hidden_done = sem("hidden_done")
        act_done = sem("act_done")
        score_done = sem("score_done")
        logits_read = sem("logits_read")
        mask_ready = sem("mask_ready")
        logits_masked = sem("logits_masked")
        max_done = sem("max_done")
        exp_done = sem("exp_done")
        inv_done = sem("inv_done")
        probs_done = sem("probs_done")
        probs_out = sem("probs_out")
        probs_in = [sem(f"probs_in{x}") for x in range(2 * GT)]
        poolw_done = sem("poolw_done")
        part_done = sem("part_done")
        parts_done = sem("parts_done")
        pooled_done = sem("pooled_done")
        pooled_moved = sem("pooled_moved")
        out_done = [sem(f"out_done{x}") for x in range(2)]

        PARAMS = 9 * 16

        block = ctx.enter_context(nc.Block())

        @block.sync
        def _(sp):
            def load_keys(n, s):
                sp.dma_start(keys[:, s, :], k_tiles[n]).then_inc(keys_in[s], 16)

            def load_mask(g, x):
                for c in range(QUADS):
                    sp.dma_start(masks[QP * c:QP * c + HALF_Q, x, :],
                                 mask_rows[g, c]).then_inc(mask_in[x], 16)

            sp.dma_start(w1[:], W1.rearrange("(c p) h -> p c h", p=P)).then_inc(params_in, 16)
            sp.dma_start(al[:], alpha.rearrange("(a b) -> a b", b=1).broadcast_to([P, 1])).then_inc(params_in, 16)
            sp.dma_start(b2c[:], b2.rearrange("(a b) -> a b", b=1).broadcast_to([P, 1])).then_inc(params_in, 16)
            for r in range(2):
                sp.dma_start(b1c[H * r:H * r + H, :], b1.rearrange("(a b) -> a b", b=1)).then_inc(params_in, 16)
                sp.dma_start(w2c[H * r:H * r + H, :], W2).then_inc(params_in, 16)
            q_v = r_q.rearrange("(t p) d -> p t d", p=P)
            for h in range(2):
                sp.dma_start(q_sb[:, 8 * h:8 * h + 8, :], q_v[:, 8 * h:8 * h + 8, :]).then_inc(params_in, 16)
            for n in range(SLOTS):
                load_keys(n, n)
                if n == 2:
                    sp.wait_ge(zeroed, 1)
                    load_mask(0, 0)
                    load_mask(1, 1)

            def step(it, s):
                n = tile_at(it, s)[0]
                if s % GT == 2 and inside(n, GT, TILES - GT):
                    g, x = tile_at(it, s)[2] + 1, (s // GT + 1) % 2
                    ge(sp, mask_ready, g - 1)
                    sp.wait_ge(zeroed, 1)
                    load_mask(g, x)
                if inside(n, LAG, TILES - SLOTS + LAG):
                    ge(sp, products_done, n - LAG + 1)
                    ge(sp, part_done, n - LAG + 1)
                    load_keys(n - LAG + SLOTS, (s - LAG) % SLOTS)
                if (s - LAG - 1) % GT == GT - 1 and inside(n, LAG + GT, TILES + LAG + 1):
                    g, x = tile_at(it, s, LAG + 1)[2], (s - LAG - 1) % SLOTS // GT
                    ge(sp, pooled_moved, g + 1)
                    sp.dma_start(out_rows[g], pooled[:, x, :].rearrange("p (s d) -> p s d", s=GT)
                                 ).then_inc(out_done[x], 16)

            run_steps(sp, step)
            for x in range(2):
                sp.wait_ge(out_done[x], 16 * (GROUPS // 2))

        @block.gpsimd
        def _(pool):
            g_ = nc.gpsimd
            g_.memset(ident[:], 0.0).then_inc(consts_base, 1)
            g_.memset(own_b[:], 1.0).then_inc(consts_base, 1)
            g_.memset(quad_b[:], 0.0).then_inc(consts_base, 1)
            g_.memset(neg[:], NEG).then_inc(consts_done, 1)
            pool.wait_ge(consts_base, 3)
            g_.affine_select(out=ident[:], in_=ident[:], compare_op=ALU.not_equal, fill=1.0, base=0,
                             pattern=[[-1, P]], channel_multiplier=1).then_inc(consts_done, 1)
            g_.affine_select(out=own_b[:], in_=own_b[:], compare_op=ALU.is_ge, fill=0.0, base=0,
                             pattern=[[-KP, SUB]], channel_multiplier=1).then_inc(consts_base, 1)
            pool.wait_ge(consts_base, 4)
            g_.affine_select(out=own_b[:], in_=own_b[:], compare_op=ALU.is_ge, fill=0.0, base=KP - 1,
                             pattern=[[KP, SUB]], channel_multiplier=-1).then_inc(consts_done, 1)
            for c in range(QUADS):
                if c:
                    pool.wait_ge(consts_base, 4 + c)
                g_.affine_select(out=quad_b[:], in_=quad_b[:], compare_op=ALU.not_equal, fill=1.0,
                                 base=-QP * c, pattern=[[-1, SUB]], channel_multiplier=1
                                 ).then_inc(consts_base if c < QUADS - 1 else consts_done, 1)
            pool.wait_ge(fold, 7)
            pool.wait_ge(qT_done, B // P // BATCH)
            pool.wait_ge(consts_done, 4)

            def weights(n, x):
                if isinstance(n, int):
                    q_n = qT[:, n * SUB:(n + 1) * SUB]
                else:
                    q_n = qT[:, bass.ds(n * SUB, SUB)]
                ge(pool, weff_done, n)
                g_.tensor_tensor(weff_q[:], q_n.unsqueeze(2).broadcast_to([P, SUB, H]),
                                 wp_f[:].unsqueeze(1).broadcast_to([P, SUB, H]), ALU.mult
                                 ).then_inc(weffq_done, 1)
                ge(pool, weffq_done, n + 1)
                ge(pool, main_done, (n - 1) * PHASES)
                g_.tensor_tensor(weff[:, x, :, :], weff_q[:], wk_f[:].unsqueeze(1).broadcast_to([P, SUB, H]),
                                 ALU.add).then_inc(weff_done, 1)

            weights(0, 0)

            def step(it, s):
                n = tile_at(it, s)[0]
                if inside(n, LAG, TILES + LAG):
                    m, ms, _, sg = tile_at(it, s, LAG)
                    x = ms // GT % 2
                    pool.wait_ge(probs_in[GT * x + sg], (round_of(it, s, LAG) + 1) * 16)
                    ge(pool, part_done, m - 1)
                    v = by_dve(m, ms)
                    g_.tensor_tensor(pool_w[:, ms % 2, 0:J - v, :],
                                     probs_k[:, x, sg, v:J].unsqueeze(2).broadcast_to([P, J - v, SUB]),
                                     own_b[:].unsqueeze(1).broadcast_to([P, J - v, SUB]), ALU.mult
                                     ).then_inc(poolw_done, 1)
                if inside(n, 0, TILES - 1):
                    weights(n + 1, (s + 1) % 2)
            run_steps(pool, step)

        @block.scalar
        def _(act_e):
            a_ = nc.scalar
            def hidden_pairs(n, s, q):
                ge(act_e, main_done, n * PHASES + q + 1)
                for k in range(2):
                    u = 2 * q + k
                    a, v = u // (PAIRS // 2), u % (PAIRS // 2)
                    if v == 0:
                        ge(act_e, act_done, 2 * n + a - 1)
                    if isinstance(n, int):
                        bias_u = bias[:, n * PAIRS + u:n * PAIRS + u + 1]
                    else:
                        bias_u = bias[:, bass.ds(n * PAIRS + u, 1)]
                    a_.activation(hidden[:, a, v, :], hP[q % 2][:, k * L:(k + 1) * L], ACT.Identity,
                                  bias=bias_u).then_inc(hidden_done, 1)

            def move_batch(n, s, b):
                if b == 0:
                    ge(act_e, main_done, (n - 1) * PHASES)
                ge(act_e, trans_done, n * NB + b + 1)
                j0, j1 = BATCHES[b]
                a_.activation(keysT[:, s % 2, j0 * P:j1 * P], trP[BANK[b]][:, 0:(j1 - j0) * P],
                              ACT.Copy).then_inc(keysT_done, 1)

            for b in range(NB):
                move_batch(0, 0, b)
            act_e.wait_ge(fold, 9)

            def step(it, s):
                n = tile_at(it, s)[0]
                if inside(n, LAG + 1, TILES + LAG + 1):
                    m, ms, _, _ = tile_at(it, s, LAG + 1)
                    ge(act_e, part_done, m + 1)
                    ge(act_e, pooled_done, m - 1)
                    a_.activation(parts[:, ms % 2, :], partP[:, 0:D], ACT.Copy).then_inc(parts_done, 1)
                for q in range(PHASES):
                    if inside(n, 0, TILES - 1):
                        for b in PHASE_BATCHES[q]:
                            move_batch(n + 1, (s + 1) % SLOTS, b)
                    scored = s % GT == 0 and inside(n, GT, TILES + 1)
                    g, x = tile_at(it, s, GT)[2], (s // GT + 1) % 2
                    if q == 2 and scored:
                        ge(act_e, poolw_done, (g - 1) * GT)
                        ge(act_e, products_done, (g - 1) * GT)
                        ge(act_e, probs_done, g + 1)
                        act_e.dma_start(probs_dram[x], probs[:, x, :]).then_inc(probs_out, 16)
                    if q == 1 and scored:
                        ge(act_e, max_done, g + 1)
                        ge(act_e, probs_done, g)
                        a_.activation(expd[:], logits[:], ACT.Exp, bias=neg_max[:], accum_out=exp_sum[:]
                                      ).then_inc(exp_done, 1)
                    if inside(n, 0, TILES):
                        hidden_pairs(n, s, q)
                    t = q + 1 if s % GT == 1 else 0
                    if (q == 3 and scored) or (t in range(1, GT) and inside(n, GT, TILES + GT)):
                        g, x = tile_at(it, s, GT)[2], (s // GT + 1) % 2
                        if t == 0:
                            ge(act_e, probs_out, (g + 1) * 16)
                        act_e.dma_start(probs_k[:, x, t, :], probs_tiles[x, t]
                                        ).then_inc(probs_in[GT * x + t], 16)
                    if q == 2 and (s - LAG - 1) % GT == GT - 1 and inside(n, LAG + GT, TILES + LAG + 1):
                        _, ms, g, _ = tile_at(it, s, LAG + 1)
                        x = ms // GT % 2
                        ge(act_e, pooled_done, (g + 1) * GT)
                        ge(act_e, out_done[x], round_of(it, s, LAG + 1) * 16)
                        a_.activation(pooled[:, x, :], pooledP[0:SUB, :], ACT.Copy).then_inc(pooled_moved, 1)

            run_steps(act_e, step)

        @block.vector
        def _(dve):
            v_ = nc.vector
            v_.memset(scoreP[:], 0.0)
            v_.memset(partP[:], 0.0)
            v_.memset(w2win[:], 0.0).then_inc(fold, 1)
            v_.memset(masks[:].rearrange("p a l -> p (a l)"), 0).then_inc(zeroed, 1)
            dve.wait_ge(params_in, PARAMS)
            v_.tensor_scalar(sgn2[:], al[:], 1.0, 2.0, ALU.is_le, ALU.mult).then_inc(fold, 1)
            v_.tensor_tensor(wsum[:, 0, :], w1[:, 0, :], w1[:, 2, :], ALU.add).then_inc(fold, 1)
            v_.tensor_tensor(wsum[:, 1, :], w1[:, 1, :], w1[:, 2, :], ALU.subtract).then_inc(fold, 1)
            dve.wait_ge(fold, 4)
            v_.tensor_scalar(sgn[:], sgn2[:], 1.0, None, ALU.subtract).then_inc(fold, 1)
            dve.wait_ge(fold, 5)
            v_.tensor_scalar(wq_f[:], wsum[:, 0, :], sgn[:], None, ALU.mult)
            v_.tensor_scalar(wk_f[:], wsum[:, 1, :], sgn[:], None, ALU.mult)
            v_.tensor_scalar(wp_f[:], w1[:, 3, :], sgn[:], None, ALU.mult)
            v_.tensor_scalar(b1s[:], b1c[:], sgn[:], None, ALU.mult)
            for r in range(2):
                v_.tensor_scalar(w2win[H * r:H * r + H, HALF_Q - 2 + r:HALF_Q - 1 + r],
                                 w2c[H * r:H * r + H, :], sgn[H * r:H * r + H, :], None, ALU.mult
                                 ).then_inc(fold, 1)
            for t in range(B // P // BATCH):
                dve.wait_ge(qT_trans, t + 1)
                v_.tensor_copy(qT[:, t * BATCH * P:(t + 1) * BATCH * P], trP[t % 2][:]).then_inc(qT_done, 1)
            for c in range(2):
                dve.wait_ge(bias_mm, c + 1)
                v_.tensor_scalar(bias[:, c * 512:(c + 1) * 512], hP[c][:], b1s[:], None, ALU.add
                                 ).then_inc(fold, 1)
            dve.wait_ge(fold, 9)

            def activate(n, s, a):
                ge(dve, hidden_done, (2 * n + a + 1) * (PAIRS // 2))
                ge(dve, score_done, 2 * n + a - 1)
                h_ = hidden[:, a, :, :].rearrange("p v l -> p (v l)")
                v_.scalar_tensor_tensor(act[:, a, :, :].rearrange("p v l -> p (v l)"), h_, al[:], h_,
                                        ALU.mult, ALU.max).then_inc(act_done, 1)

            def mask_scores(g, x):
                ge(dve, score_done, (g + 1) * (2 * GT))
                ge(dve, exp_done, g)
                v_.tensor_scalar(logits[:].rearrange("p (i j) -> p j i", i=KP),
                                 scoreP[:, 0:L].rearrange("p (j i) -> p j i", i=KP), b2c[:], None, ALU.add
                                 ).then_inc(logits_read, 1)
                dve.wait_ge(consts_done, 1)
                ge(dve, logits_read, g + 1)
                ge(dve, mask_ready, g + 1)
                v_.copy_predicated(logits[:], masked[:, x, :], neg[:]).then_inc(logits_masked, 1)
                ge(dve, logits_masked, g + 1)
                v_.tensor_reduce(neg_max[:], logits[:], AX_X, ALU.max, negate=True).then_inc(max_done, 1)

            def normalise(g, x):
                ge(dve, exp_done, g + 1)
                v_.reciprocal(inv_sum[:], exp_sum[:]).then_inc(inv_done, 1)
                ge(dve, inv_done, g + 1)
                ge(dve, probs_out, (g - 1) * 16)
                v_.tensor_scalar(probs[:, x, :], expd[:], inv_sum[:], None, ALU.mult).then_inc(probs_done, 1)

            def multiply(it, s):
                m, ms, _, sg = tile_at(it, s, LAG)
                x, v = ms // GT, by_dve(m, ms)
                dve.wait_ge(probs_in[GT * x + sg], (round_of(it, s, LAG) + 1) * 16)
                dve.wait_ge(keys_in[ms], (round_of(it, s, LAG) + 1) * 16)
                ge(dve, parts_v_done, m)
                v_.tensor_tensor(products[:, 0:v * D].rearrange("p (j d) -> p j d", d=D),
                                 keys[:, ms, 0:v * D].rearrange("p (j d) -> p j d", d=D),
                                 probs_k[:, x, sg, 0:v].unsqueeze(2).broadcast_to([P, v, D]), ALU.mult
                                 ).then_inc(products_done, 1)

            def add_products(m, ms):
                ge(dve, products_done, m + 1)
                ge(dve, pooled_done, m - 1)
                v_.tensor_reduce(parts_v[:, ms % 2, :], products[:, 0:by_dve(m, ms) * D].rearrange("p (j d) -> p d j", d=D),
                                 AX_X, ALU.add).then_inc(parts_v_done, 1)

            def step(it, s):
                n = tile_at(it, s)[0]
                scored = s % GT == 0 and inside(n, GT, TILES + 1)
                g, x = tile_at(it, s, GT)[2], (s // GT + 1) % 2
                for q in range(PHASES):
                    if q == 0 and scored:
                        mask_scores(g, x)
                    if inside(n, LAG, TILES + LAG):
                        if q == (2 if scored else 0):
                            multiply(it, s)
                        if q == 2 and not scored:
                            add_products(*tile_at(it, s, LAG)[:2])
                    if q == 1 and scored:
                        normalise(g, x)
                    if q % 2 and inside(n, 0, TILES):
                        activate(n, s, q // 2)
                    if q == 3 and scored and inside(n, LAG, TILES + LAG):
                        add_products(*tile_at(it, s, LAG)[:2])
                    if q == 2 and s % GT == 1 and inside(n, 0, TILES):
                        dve.wait_ge(mask_in[s // GT], (it + 1) * (16 * QUADS))
                        ge(dve, logits_masked, tile_at(it, s)[2] - 1)
                        v_.tensor_scalar(masked[:, s // GT, :], masks[:, s // GT, :], 0, None, ALU.is_equal
                                         ).then_inc(mask_ready, 1)

            run_steps(dve, step)

        @block.tensor
        def _(pe):
            t_ = nc.tensor
            pe.wait_ge(params_in, PARAMS)
            pe.wait_ge(consts_done, 4)
            for t in range(B // P):
                if t % BATCH == 0 and t >= 2 * BATCH:
                    pe.wait_ge(qT_done, t // BATCH - 1)
                mm = t_.transpose(trP[t // BATCH % 2][:, t % BATCH * P:(t % BATCH + 1) * P], q_sb[:, t, :],
                                  ident[:])
                if t % BATCH == BATCH - 1:
                    mm.then_inc(qT_trans, 1)
            pe.wait_ge(fold, 7)
            pe.wait_ge(qT_done, B // P // BATCH)
            for c in range(2):
                for r in range(2):
                    mm = t_.matmul(hP[c][H * r:H * r + H, :], wq_f[:],
                                   qT[:, 1024 * c:1024 * (c + 1)].rearrange("p (n c a r) -> p r n a c", c=QUADS, a=2, r=2)[:, r],
                                   start=True, stop=True)
                mm.then_inc(bias_mm, 1)

            def transpose_batch(n, s, rnd, b):
                if b == 0:
                    pe.wait_ge(keys_in[s], (rnd + 1) * 16)
                last = [x for x in range(-NB, b) if BANK[x % NB] == BANK[b]][-1]
                ge(pe, keysT_done, n * NB + last + 1)
                j0, j1 = BATCHES[b]
                for j in range(j0, j1):
                    mm = t_.transpose(trP[BANK[b]][:, (j - j0) * P:(j - j0 + 1) * P],
                                      keys[:, s, j * D:(j + 1) * D], ident[:])
                mm.then_inc(trans_done, 1)

            def first_layer(n, s, q):
                if q == 0:
                    ge(pe, keysT_done, (n + 1) * NB)
                    ge(pe, weff_done, n + 1)
                ge(pe, hidden_done, 2 * (n * PHASES + q - 1))
                kT = keysT[:, s % 2, :].rearrange("p (j c) -> p j c", j=J)
                for k in range(2):
                    for r in range(2):
                        b = 4 * (2 * (q % 2) + k) + 2 * (q // 2) + r
                        mm = t_.matmul(hP[q % 2][H * r:H * r + H, k * L:(k + 1) * L], weff[:, s % 2, b, :],
                                       kT[:, :, b * KP:(b + 1) * KP], start=True, stop=True)
                mm.then_inc(main_done, 1)

            def second_layer(n, s, g, a):
                ge(pe, act_done, 2 * n + a + 1)
                if s % GT == 0 and a == 0:
                    ge(pe, logits_read, g)
                t = 2 * (s % GT) + a
                for c in range(QUADS):
                    mm = t_.matmul(scoreP[QP * c:QP * c + HALF_Q, 0:L],
                                   w2win[:, HALF_Q - 2 - 2 * t:2 * HALF_Q - 2 - 2 * t],
                                   act[:, a, c, :], start=(t == 0), stop=(t == 2 * GT - 1))
                mm.then_inc(score_done, 1)

            def pool_keys(m, ms, q):
                if q == 1:
                    ge(pe, poolw_done, m + 1)
                    ge(pe, parts_done, m)
                v = by_dve(m, ms)
                for j in range(v if q == 1 else J - (PHASES - q) * QUADS, J - (PHASES - 1 - q) * QUADS):
                    c = (j - v) % QUADS
                    mm = t_.matmul(partP[QP * c:QP * c + SUB, 0:D], pool_w[:, ms % 2, j - v, :],
                                   keys[:, ms, j * D:(j + 1) * D], start=(j - v < QUADS),
                                   stop=(j + QUADS >= J))
                if q == PHASES - 1:
                    mm.then_inc(part_done, 1)

            def add_parts(m, ms, g):
                ge(pe, parts_done, m + 1)
                if ms % GT == 0:
                    ge(pe, pooled_moved, g)
                sums = pooledP[0:SUB, (ms % GT) * D:(ms % GT + 1) * D]
                t_.matmul(sums, quad_b[:], parts[:, ms % 2, :], start=True, stop=False)
                ge(pe, parts_v_done, m + 1)
                t_.matmul(sums, own_b[:], parts_v[:, ms % 2, :], start=False, stop=True
                          ).then_inc(pooled_done, 1)

            for b in range(NB):
                transpose_batch(0, 0, 0, b)
            pe.wait_ge(fold, 9)

            def step(it, s):
                n = tile_at(it, s)[0]
                for q in range(PHASES):
                    if inside(n, 0, TILES - 1):
                        for b in PHASE_BATCHES[q]:
                            transpose_batch(n + 1, (s + 1) % SLOTS, round_of(it, s, -1), b)
                    if inside(n, 0, TILES):
                        first_layer(n, s, q)
                    if q == 1 and inside(n, LAG + 1, TILES + LAG + 1):
                        add_parts(*tile_at(it, s, LAG + 1)[:3])
                    if q > 0 and inside(n, LAG, TILES + LAG):
                        pool_keys(n - LAG, (s - LAG) % SLOTS, q)
                    if q == 0 and inside(n, 1, TILES + 1):
                        second_layer(n - 1, (s - 1) % SLOTS, tile_at(it, s, 1)[2], 1)
                    if q == 3 and inside(n, 0, TILES):
                        second_layer(n, s, tile_at(it, s)[2], 0)

            run_steps(pe, step)


_INS = ["r_q", "r_k", "r_mask", "L0_rec_W1", "L0_rec_b1", "L0_rec_alpha", "L0_rec_W2", "L0_rec_b2"]


def kernel(**inputs):
    import numpy as np
    import concourse.bacc as bacc
    from concourse.bass_utils import run_bass_kernel_spmd

    nc = bacc.Bacc("TRN2", target_bir_lowering=False, num_devices=1)
    arrays, args = {}, []
    for name in _INS:
        a = np.ascontiguousarray(inputs[name])
        arrays[f"in_{name}"] = a
        args.append(nc.dram_tensor(f"in_{name}", a.shape, mybir.dt.from_np(a.dtype), kind="ExternalInput").ap())
    args.append(nc.dram_tensor("out_rows", (B, D), F32, kind="ExternalOutput").ap())
    attention_pooling(nc, *args)
    r = run_bass_kernel_spmd(nc, [arrays], core_ids=[0])
    return r.results[0]["out_rows"]
```
